# Optimizing a Trainium2 kernel written in Bass

```python
import numpy as np
import jax
import jax.numpy as jnp

def _softmax(x, axis=-1):
    return jax.nn.softmax(x, axis=axis)

def _gelu(x):
    return jax.nn.gelu(x, approximate=True)

def _silu(x):
    return jax.nn.silu(x)

def _sigmoid(x):
    return jax.nn.sigmoid(x)

def _layernorm(x, axis=-1, eps=1e-05):
    m = jnp.mean(x, axis=axis, keepdims=True)
    v = jnp.var(x, axis=axis, keepdims=True)
    return (x - m) / jnp.sqrt(v + eps)

def _scatter_add(tgt, idx, src, axis=0):
    return tgt.at[idx].add(src)

def _segment_sum(src, seg, n):
    return jax.ops.segment_sum(src, seg, n)
kernel_name = 'mk_dlrm_tower_d1_rec_r8_8ceab6'

def setup_inputs(seed: int=0):
    np.random.seed(seed)
    _w = jnp.asarray

    def _rec_inputs():
        import jax
        import jax.numpy as jnp
        _tk = jax.random.key(seed)
        dense_ctx = jax.random.normal(jax.random.fold_in(_tk, 190), (512, 16), jnp.float32)
        ids = jnp.stack([jax.random.randint(jax.random.fold_in(_tk, 200 + f), (512,), 0, v, jnp.int32) for f, v in enumerate([1250, 1250, 1000, 1000, 125000, 12500, 1000, 1000, 1250, 12500, 1000, 1000, 12500, 1250, 12500, 1000, 12500, 12500, 1000, 1250, 1250, 1000, 12500, 1250, 12500, 1000, 1250])], axis=1)
        tbl_0 = 0.05 * jax.random.normal(jax.random.fold_in(_tk, 500 + 0), (1250, 128), jnp.float32)
        tbl_1 = 0.05 * jax.random.normal(jax.random.fold_in(_tk, 500 + 1), (1250, 128), jnp.float32)
        tbl_2 = 0.05 * jax.random.normal(jax.random.fold_in(_tk, 500 + 2), (1000, 128), jnp.float32)
        tbl_3 = 0.05 * jax.random.normal(jax.random.fold_in(_tk, 500 + 3), (1000, 128), jnp.float32)
        tbl_4 = 0.05 * jax.random.normal(jax.random.fold_in(_tk, 500 + 4), (125000, 128), jnp.float32)
        tbl_5 = 0.05 * jax.random.normal(jax.random.fold_in(_tk, 500 + 5), (12500, 128), jnp.float32)
        tbl_6 = 0.05 * jax.random.normal(jax.random.fold_in(_tk, 500 + 6), (1000, 128), jnp.float32)
        tbl_7 = 0.05 * jax.random.normal(jax.random.fold_in(_tk, 500 + 7), (1000, 128), jnp.float32)
        tbl_8 = 0.05 * jax.random.normal(jax.random.fold_in(_tk, 500 + 8), (1250, 128), jnp.float32)
        tbl_9 = 0.05 * jax.random.normal(jax.random.fold_in(_tk, 500 + 9), (12500, 128), jnp.float32)
        tbl_10 = 0.05 * jax.random.normal(jax.random.fold_in(_tk, 500 + 10), (1000, 128), jnp.float32)
        tbl_11 = 0.05 * jax.random.normal(jax.random.fold_in(_tk, 500 + 11), (1000, 128), jnp.float32)
        tbl_12 = 0.05 * jax.random.normal(jax.random.fold_in(_tk, 500 + 12), (12500, 128), jnp.float32)
        tbl_13 = 0.05 * jax.random.normal(jax.random.fold_in(_tk, 500 + 13), (1250, 128), jnp.float32)
        tbl_14 = 0.05 * jax.random.normal(jax.random.fold_in(_tk, 500 + 14), (12500, 128), jnp.float32)
        tbl_15 = 0.05 * jax.random.normal(jax.random.fold_in(_tk, 500 + 15), (1000, 128), jnp.float32)
        tbl_16 = 0.05 * jax.random.normal(jax.random.fold_in(_tk, 500 + 16), (12500, 128), jnp.float32)
        tbl_17 = 0.05 * jax.random.normal(jax.random.fold_in(_tk, 500 + 17), (12500, 128), jnp.float32)
        tbl_18 = 0.05 * jax.random.normal(jax.random.fold_in(_tk, 500 + 18), (1000, 128), jnp.float32)
        tbl_19 = 0.05 * jax.random.normal(jax.random.fold_in(_tk, 500 + 19), (1250, 128), jnp.float32)
        tbl_20 = 0.05 * jax.random.normal(jax.random.fold_in(_tk, 500 + 20), (1250, 128), jnp.float32)
        tbl_21 = 0.05 * jax.random.normal(jax.random.fold_in(_tk, 500 + 21), (1000, 128), jnp.float32)
        tbl_22 = 0.05 * jax.random.normal(jax.random.fold_in(_tk, 500 + 22), (12500, 128), jnp.float32)
        tbl_23 = 0.05 * jax.random.normal(jax.random.fold_in(_tk, 500 + 23), (1250, 128), jnp.float32)
        tbl_24 = 0.05 * jax.random.normal(jax.random.fold_in(_tk, 500 + 24), (12500, 128), jnp.float32)
        tbl_25 = 0.05 * jax.random.normal(jax.random.fold_in(_tk, 500 + 25), (1000, 128), jnp.float32)
        tbl_26 = 0.05 * jax.random.normal(jax.random.fold_in(_tk, 500 + 26), (1250, 128), jnp.float32)
        _rk = jax.random.fold_in(_tk, 7)
        W_top1 = 0.0521996 * jax.random.normal(jax.random.fold_in(_tk, 801), (367, 512), jnp.float32)
        W_top2 = 0.0441942 * jax.random.normal(jax.random.fold_in(_tk, 802), (512, 256), jnp.float32)
        W_top3 = 0.0625 * jax.random.normal(jax.random.fold_in(_tk, 803), (256, 1), jnp.float32)
        b_top1 = jnp.zeros((512,), jnp.float32)
        b_top2 = jnp.zeros((256,), jnp.float32)
        return (dense_ctx, ids, tbl_0, tbl_1, tbl_2, tbl_3, tbl_4, tbl_5, tbl_6, tbl_7, tbl_8, tbl_9, tbl_10, tbl_11, tbl_12, tbl_13, tbl_14, tbl_15, tbl_16, tbl_17, tbl_18, tbl_19, tbl_20, tbl_21, tbl_22, tbl_23, tbl_24, tbl_25, tbl_26, W_top1, b_top1, W_top2, b_top2, W_top3)
    dense_ctx, ids, tbl_0, tbl_1, tbl_2, tbl_3, tbl_4, tbl_5, tbl_6, tbl_7, tbl_8, tbl_9, tbl_10, tbl_11, tbl_12, tbl_13, tbl_14, tbl_15, tbl_16, tbl_17, tbl_18, tbl_19, tbl_20, tbl_21, tbl_22, tbl_23, tbl_24, tbl_25, tbl_26, W_top1, b_top1, W_top2, b_top2, W_top3 = _rec_inputs()

    def _L0_rec_setup():
        import jax, jax.numpy as jnp
        import numpy as np

        def _tri_indices(num_feas):
            return np.array([i * num_feas + j for j in range(1, num_feas) for i in range(j)], dtype=np.int32)
        key = jax.random.key(seed)
        batch, num_feas, embed_dim = (2048, 27, 128)
        inputs = jax.random.normal(key, (batch, num_feas, embed_dim), dtype=jnp.float32)
        return {'inputs': inputs, 'num_feas': num_feas}
    _L0_rec_all = _L0_rec_setup()
    _L0_rec_in = {k: v for k, v in _L0_rec_all.items() if k in ()}
    del _L0_rec_all
    return {'dense_ctx': dense_ctx, 'ids': ids, 'tbl_0': tbl_0, 'tbl_1': tbl_1, 'tbl_2': tbl_2, 'tbl_3': tbl_3, 'tbl_4': tbl_4, 'tbl_5': tbl_5, 'tbl_6': tbl_6, 'tbl_7': tbl_7, 'tbl_8': tbl_8, 'tbl_9': tbl_9, 'tbl_10': tbl_10, 'tbl_11': tbl_11, 'tbl_12': tbl_12, 'tbl_13': tbl_13, 'tbl_14': tbl_14, 'tbl_15': tbl_15, 'tbl_16': tbl_16, 'tbl_17': tbl_17, 'tbl_18': tbl_18, 'tbl_19': tbl_19, 'tbl_20': tbl_20, 'tbl_21': tbl_21, 'tbl_22': tbl_22, 'tbl_23': tbl_23, 'tbl_24': tbl_24, 'tbl_25': tbl_25, 'tbl_26': tbl_26, 'W_top1': W_top1, 'b_top1': b_top1, 'W_top2': W_top2, 'b_top2': b_top2, 'W_top3': W_top3}

def reference(dense_ctx, ids, tbl_0, tbl_1, tbl_2, tbl_3, tbl_4, tbl_5, tbl_6, tbl_7, tbl_8, tbl_9, tbl_10, tbl_11, tbl_12, tbl_13, tbl_14, tbl_15, tbl_16, tbl_17, tbl_18, tbl_19, tbl_20, tbl_21, tbl_22, tbl_23, tbl_24, tbl_25, tbl_26, W_top1, b_top1, W_top2, b_top2, W_top3):
    import jax
    import jax.numpy as jnp

    def _L0_rec_ref(inputs, num_feas):
        import jax, jax.numpy as jnp
        import numpy as np

        def _tri_indices(num_feas):
            return np.array([i * num_feas + j for j in range(1, num_feas) for i in range(j)], dtype=np.int32)
        dot = jnp.einsum('bnd,bmd->bnm', inputs, inputs)
        idx = jnp.asarray(_tri_indices(num_feas))
        flat = dot.reshape(inputs.shape[0], num_feas * num_feas)
        return flat[:, idx]
    e = jnp.stack([tbl_0[ids[:, 0]], tbl_1[ids[:, 1]], tbl_2[ids[:, 2]], tbl_3[ids[:, 3]], tbl_4[ids[:, 4]], tbl_5[ids[:, 5]], tbl_6[ids[:, 6]], tbl_7[ids[:, 7]], tbl_8[ids[:, 8]], tbl_9[ids[:, 9]], tbl_10[ids[:, 10]], tbl_11[ids[:, 11]], tbl_12[ids[:, 12]], tbl_13[ids[:, 13]], tbl_14[ids[:, 14]], tbl_15[ids[:, 15]], tbl_16[ids[:, 16]], tbl_17[ids[:, 17]], tbl_18[ids[:, 18]], tbl_19[ids[:, 19]], tbl_20[ids[:, 20]], tbl_21[ids[:, 21]], tbl_22[ids[:, 22]], tbl_23[ids[:, 23]], tbl_24[ids[:, 24]], tbl_25[ids[:, 25]], tbl_26[ids[:, 26]]], axis=1)
    z = _L0_rec_ref(e, 27)
    z = z.reshape(z.shape[0], -1)
    h = jnp.concatenate([z, dense_ctx], axis=1)
    h = jnp.maximum(h @ W_top1 + b_top1, 0.0)
    h = jnp.maximum(h @ W_top2 + b_top2, 0.0)
    y = h @ W_top3
    return y

_drawn_inputs = setup_inputs


def setup_inputs(seed=0):
    import zlib

    import numpy as np

    out = dict(_drawn_inputs(seed))
    spreads = {'b_top1': (0.0, 0.1), 'b_top2': (0.0, 0.1)}
    factors = {}
    for name, (base, spread) in spreads.items():
        noise = np.random.default_rng([zlib.crc32(name.encode()), seed]).standard_normal(out[name].shape)
        drawn = base * np.exp(spread * noise) if base else spread * noise
        out[name] = jnp.asarray(drawn.astype(out[name].dtype))
    for name, factor in factors.items():
        out[name] = (out[name] * factor).astype(out[name].dtype)
    return out
```

```python
import numpy as np

TABLE_ROWS = [1250, 1250, 1000, 1000, 125000, 12500, 1000, 1000, 1250, 12500, 1000, 1000, 12500, 1250,
              12500, 1000, 12500, 12500, 1000, 1250, 1250, 1000, 12500, 1250, 12500, 1000, 1250]
FEATURES = len(TABLE_ROWS)
BATCH, EMBED, DENSE, HID1, HID2 = 512, 128, 16, 512, 256

PICKED_ROWS = 1000
PICKED = [f for f, rows in enumerate(TABLE_ROWS) if rows == PICKED_ROWS][:7]
FETCHED = [f for f in range(FEATURES) if f not in PICKED]
SLOTS = FETCHED + PICKED
PICKS = len(PICKED)

QUAD = 32
GROUP = 32
GROUPS = BATCH // GROUP
PER_FETCH = 128 // GROUP
FETCHES = len(FETCHED) // PER_FETCH
TILE = 128
TILES = BATCH // TILE
GROUPS_PER_TILE = TILE // GROUP
SET = 4
SETS = GROUP // SET
STEPS = 7
PICK_K = 125
PICK_CHUNKS = PICKED_ROWS // PICK_K
CHUNKS1, CHUNKS2 = HID1 // 128, HID2 // 128
RAW_RING = 6
TABLE_RING = 2


def plan():
    order = []
    for n in range(PICKS):
        order.append(("pick", n))
        if n >= 1:
            order.append(("turn", n - 1))
    turned = PICKS - 1
    after = []
    for g in range(GROUPS):
        while turned < GROUPS and turned <= g + max(1, 6 - g // 2):
            order.append(("turn", turned))
            turned += 1
        order.append(("dots", g))
        if after:
            order.append(after.pop(0))
        if g % GROUPS_PER_TILE == GROUPS_PER_TILE - 1:
            t = g // GROUPS_PER_TILE
            after += [("layer1", t), ("layer2", t), ("layer3", t)]
    return order + after


def build(nc, table, fetch_ids, fetch_base, pick_ids, pick_tables, pick_rows, dense, w1, b1, w2, b2, w3, y):
    import concourse.bass as bass
    from concourse import mybir
    from contextlib import ExitStack

    F32, F32R, I32 = mybir.dt.float32, mybir.dt.float32r, mybir.dt.int32
    ALU, ACT = mybir.AluOpType, mybir.ActivationFunctionType

    ctx = ExitStack()
    with ctx:
        def sb(name, shape, dt=F32):
            return ctx.enter_context(nc.sbuf_tensor(name, shape, dt))

        def pb(name, shape):
            return ctx.enter_context(nc.psum_tensor(name, shape, F32))

        def sem(name):
            return ctx.enter_context(nc.semaphore(name))

        ids_sb = sb("ids_sb", [128, GROUPS * FETCHES], I32)
        base_sb = sb("base_sb", [128, GROUPS * FETCHES], I32)
        rows_sb = sb("rows_sb", [128, GROUPS * FETCHES], I32)
        raw = sb("raw", [128, RAW_RING, FETCHES, EMBED])
        pick_ids_sb = sb("pick_ids_sb", [128, PICKS, BATCH], I32)
        pick_rows_sb = sb("pick_rows_sb", [128, PICK_CHUNKS])
        tab = sb("tab", [128, TABLE_RING, PICK_CHUNKS * EMBED])
        tab_hi = sb("tab_hi", [128, TABLE_RING, PICK_CHUNKS * EMBED], F32R)
        tab_lo = sb("tab_lo", [128, TABLE_RING, PICK_CHUNKS * EMBED], F32R)
        onehot = sb("onehot", [128, PICK_CHUNKS, BATCH], F32R)
        emb = sb("emb", [128, BATCH, QUAD])
        dots = sb("dots", [128, STEPS, BATCH])
        w1_sb = sb("w1_sb", [128, STEPS, HID1])
        w2_sb = sb("w2_sb", [128, CHUNKS1, HID2])
        w3_sb = sb("w3_sb", [128, CHUNKS2])
        b1_sb = sb("b1_sb", [128, CHUNKS1])
        b2_sb = sb("b2_sb", [128, CHUNKS2])
        ident = sb("ident", [128, 128])
        h1 = sb("h1", [128, CHUNKS1, TILE])
        h2 = sb("h2", [128, CHUNKS2, TILE])
        y_sb = sb("y_sb", [1, BATCH])

        turn_ps = pb("turn_ps", [128, 2, 512])
        dots_ps = pb("dots_ps", [128, 4, 512])
        acc_ps = pb("acc_ps", [128, 2, 512])

        ids_in = sem("ids_in")
        rows_ready = sem("rows_ready")
        ident_ready = sem("ident_ready")
        raw_in = [sem(f"raw_in{r}") for r in range(RAW_RING)]
        pick_rows_in = sem("pick_rows_in")
        pick_ids_in = [sem(f"pick_ids_in{n}") for n in range(PICKS)]
        tab_in = [sem(f"tab_in{r}") for r in range(TABLE_RING)]
        hi_ready = sem("hi_ready")
        lo_ready = sem("lo_ready")
        onehot_ready = sem("onehot_ready")
        onehot_used = sem("onehot_used")
        pick_out = sem("pick_out")
        turned_a = sem("turned_a")
        turned_b = sem("turned_b")
        turn_out_a = sem("turn_out_a")
        turn_out_b = sem("turn_out_b")
        pad_zero = sem("pad_zero")
        dense_zero = sem("dense_zero")
        dense_in = sem("dense_in")
        w1_in = sem("w1_in")
        w23_in = sem("w23_in")
        dotted = sem("dotted")
        dots_out_act = sem("dots_out_act")
        dots_out_dve = sem("dots_out_dve")
        layer1_a = sem("layer1_a")
        layer1_b = sem("layer1_b")
        h1_a = sem("h1_a")
        h1_b = sem("h1_b")
        layer2_done = sem("layer2_done")
        h2_ready = sem("h2_ready")
        layer3_done = sem("layer3_done")
        y_ready = sem("y_ready")
        y_written = sem("y_written")

        FIRST_FETCHES = 3
        order = plan()
        COLS = SET * FEATURES

        def turn_out(engine_copy, g, bank):
            a, b = (0, FIRST_FETCHES) if bank == 0 else (FIRST_FETCHES, FETCHES)
            src = turn_ps[:, bank, 0:(b - a) * 128].rearrange("p (f s) -> p f s", s=GROUP)
            dst = emb[:, g * GROUP:(g + 1) * GROUP, PER_FETCH * a:PER_FETCH * b].rearrange("p s f -> p f s")
            return engine_copy(dst, src)

        def dots_out(engine_copy, g, s):
            half = 2 * (g % 2)
            for c in range(4):
                n = STEPS if c < 3 else FEATURES - 3 * STEPS
                src = dots_ps[QUAD * s:QUAD * (s + 1), half:half + 2, 0:4 * COLS].rearrange(
                    "p b (q x) -> p b q x", q=4)[:, :, :, FEATURES * s + STEPS * c:FEATURES * s + STEPS * c + n]
                dst = dots[QUAD * c:QUAD * (c + 1), 0:n, g * GROUP:(g + 1) * GROUP].rearrange(
                    "p t (b q s) -> p b q t s", b=2, q=4)[:, :, :, :, s]
                last = engine_copy(dst, src)
            return last

        block = ctx.enter_context(nc.Block())

        @block.sync
        def _(sp):
            sp.dma_start(ids_sb[:, :], fetch_ids).then_inc(ids_in, 16)
            sp.dma_start(base_sb[:, :], fetch_base).then_inc(ids_in, 16)
            sp.dma_start(pick_rows_sb[:, :], pick_rows).then_inc(pick_rows_in, 16)
            for n in range(PICKS):
                sp.dma_start(pick_ids_sb[:, n, :], pick_ids[n:n + 1, :].broadcast_to([128, BATCH])).then_inc(pick_ids_in[n], 16)
                if n >= TABLE_RING:
                    sp.wait_ge(lo_ready, n - TABLE_RING + 1)
                    sp.wait_ge(hi_ready, n - TABLE_RING + 1)
                rows = pick_tables[n].rearrange("(p c) d -> p (c d)", c=PICK_CHUNKS)
                sp.dma_start(tab[0:120, n % TABLE_RING, :], rows[0:120, :]).then_inc(tab_in[n % TABLE_RING], 16)
                sp.dma_start(tab[120:PICK_K, n % TABLE_RING, :], rows[120:PICK_K, :]).then_inc(tab_in[n % TABLE_RING], 16)
                if n == 2:
                    sp.dma_start(w1_sb[:, :, :], w1).then_inc(w1_in, 16)
            sp.dma_start(w2_sb[:, :, :], w2.rearrange("(c p) n -> p c n", p=128)).then_inc(w23_in, 16)
            sp.dma_start(w3_sb[:, :], w3).then_inc(w23_in, 16)
            sp.dma_start(b1_sb[:, :], b1).then_inc(w23_in, 16)
            sp.dma_start(b2_sb[:, :], b2).then_inc(w23_in, 16)
            sp.wait_ge(dense_zero, 1)
            sp.dma_start(dots[3 * QUAD:3 * QUAD + DENSE, STEPS - 1, :], dense).then_inc(dense_in, 16)
            sp.wait_ge(y_ready, TILES)
            sp.dma_start(y, y_sb[:, :]).then_inc(y_written, 16)
            sp.wait_ge(y_written, 16)

        @block.gpsimd
        def _(pool):
            nc.gpsimd.memset(ident[:, :], 0.0).then_inc(ident_ready, 1)
            pool.wait_ge(ident_ready, 1)
            nc.gpsimd.affine_select(out=ident[:, :], in_=ident[:, :], compare_op=ALU.not_equal, fill=1.0, base=0,
                                    pattern=[[-1, 128]], channel_multiplier=1).then_inc(ident_ready, 1)
            pool.wait_ge(rows_ready, 1)
            for g in range(GROUPS):
                if g >= RAW_RING:
                    pool.wait_ge(turned_b, g - RAW_RING + 1)
                for k in range(FETCHES):
                    at = g * FETCHES + k
                    pool.indirect_dma_start(raw[:, g % RAW_RING, k, :], None, table,
                                            bass.IndirectOffsetOnAxis(rows_sb[:, at:at + 1], 0)).then_inc(
                                                raw_in[g % RAW_RING], 16)

        @block.vector
        def _(dve):
            dve.wait_ge(ids_in, 32)
            nc.vector.tensor_tensor(rows_sb[:, :], ids_sb[:, :], base_sb[:, :], ALU.add).then_inc(rows_ready, 1)
            nc.vector.memset(dots[3 * QUAD:4 * QUAD, STEPS - 1, :], 0.0).then_inc(dense_zero, 1)
            dve.wait_ge(pick_rows_in, 16)
            for kind, n in order:
                if kind == "pick":
                    dve.wait_ge(pick_ids_in[n], 16)
                    for c in range(PICK_CHUNKS):
                        if n >= 1:
                            dve.wait_ge(onehot_used, (n - 1) * PICK_CHUNKS + c + 1)
                        nc.vector.tensor_scalar(onehot[0:PICK_K, c, :], pick_ids_sb[0:PICK_K, n, :],
                                                pick_rows_sb[0:PICK_K, c:c + 1], None, ALU.is_equal).then_inc(onehot_ready, 1)
                        if c == 0:
                            dve.wait_ge(hi_ready, n + 1)
                            dve.wait_ge(tab_in[n % TABLE_RING], 32 * (n // TABLE_RING + 1))
                            if n >= TABLE_RING:
                                dve.wait_ge(onehot_used, PICK_CHUNKS * (n - TABLE_RING + 1))
                            nc.vector.tensor_tensor(tab_lo[0:PICK_K, n % TABLE_RING, :], tab[0:PICK_K, n % TABLE_RING, :],
                                                    tab_hi[0:PICK_K, n % TABLE_RING, :].bitcast(F32), ALU.subtract).then_inc(lo_ready, 1)
                    if n == 1:
                        nc.vector.memset(emb[:, :, FEATURES:QUAD], 0.0).then_inc(pad_zero, 1)
                elif kind == "dots":
                    dve.wait_ge(dotted, n + 1)
                    dots_out(nc.vector.tensor_copy, n, 2)
                    dots_out(nc.vector.tensor_copy, n, 3).then_inc(dots_out_dve, 1)
                elif kind == "layer1":
                    if n == 0:
                        dve.wait_ge(w23_in, 64)
                    if n >= 1:
                        dve.wait_ge(layer2_done, n)
                    dve.wait_ge(layer1_b, n + 1)
                    for m in (2, 3):
                        last = nc.vector.tensor_scalar(h1[:, m, :], acc_ps[:, 1, 128 * (m - 2):128 * (m - 1)],
                                                       b1_sb[:, m:m + 1], 0.0, ALU.add, ALU.max)
                    last.then_inc(h1_b, 1)

        @block.scalar
        def _(act):
            for kind, n in order:
                if kind == "pick":
                    act.wait_ge(tab_in[n % TABLE_RING], 32 * (n // TABLE_RING + 1))
                    if n >= TABLE_RING:
                        act.wait_ge(onehot_used, PICK_CHUNKS * (n - TABLE_RING + 1))
                    nc.scalar.copy(tab_hi[0:PICK_K, n % TABLE_RING, :], tab[0:PICK_K, n % TABLE_RING, :]).then_inc(hi_ready, 1)
                    if n >= 1:
                        act.wait_ge(onehot_used, PICK_CHUNKS * n)
                        nc.scalar.copy(emb[:, :, len(FETCHED) + n - 1], acc_ps[:, (n - 1) % 2, :]).then_inc(pick_out, 1)
                elif kind == "turn":
                    act.wait_ge(turned_a, n + 1)
                    turn_out(nc.scalar.copy, n, 0).then_inc(turn_out_a, 1)
                    act.wait_ge(turned_b, n + 1)
                    turn_out(nc.scalar.copy, n, 1).then_inc(turn_out_b, 1)
                    if n == PICKS - 2:
                        act.wait_ge(onehot_used, PICK_CHUNKS * PICKS)
                        nc.scalar.copy(emb[:, :, FEATURES - 1], acc_ps[:, (PICKS - 1) % 2, :]).then_inc(pick_out, 1)
                elif kind == "dots":
                    act.wait_ge(dotted, n + 1)
                    dots_out(nc.scalar.copy, n, 0)
                    dots_out(nc.scalar.copy, n, 1).then_inc(dots_out_act, 1)
                elif kind == "layer1":
                    if n == 0:
                        act.wait_ge(w23_in, 64)
                    if n >= 1:
                        act.wait_ge(layer2_done, n)
                    act.wait_ge(layer1_a, n + 1)
                    for m in (0, 1):
                        last = nc.scalar.activation(h1[:, m, :], acc_ps[:, 0, 128 * m:128 * (m + 1)], ACT.Relu,
                                                    bias=b1_sb[:, m:m + 1])
                    last.then_inc(h1_a, 1)
                elif kind == "layer2":
                    if n >= 1:
                        act.wait_ge(layer3_done, n)
                    act.wait_ge(layer2_done, n + 1)
                    for m in range(CHUNKS2):
                        last = nc.scalar.activation(h2[:, m, :], acc_ps[:, 0, 128 * m:128 * (m + 1)], ACT.Relu,
                                                    bias=b2_sb[:, m:m + 1])
                    last.then_inc(h2_ready, 1)
                else:
                    act.wait_ge(layer3_done, n + 1)
                    nc.scalar.copy(y_sb[:, n * TILE:(n + 1) * TILE], acc_ps[0:1, 1, 0:TILE]).then_inc(y_ready, 1)

        @block.tensor
        def _(pe):
            for kind, n in order:
                if kind == "pick":
                    pe.wait_ge(hi_ready, n + 1)
                    pe.wait_ge(lo_ready, n + 1)
                    if n >= 2:
                        pe.wait_ge(pick_out, n - 1)
                    for c in range(PICK_CHUNKS):
                        pe.wait_ge(onehot_ready, n * PICK_CHUNKS + c + 1)
                        nc.tensor.matmul(acc_ps[:, n % 2, :], tab_hi[0:PICK_K, n % TABLE_RING, EMBED * c:EMBED * (c + 1)],
                                         onehot[0:PICK_K, c, :], start=c == 0, stop=False)
                        last = nc.tensor.matmul(acc_ps[:, n % 2, :], tab_lo[0:PICK_K, n % TABLE_RING, EMBED * c:EMBED * (c + 1)],
                                                onehot[0:PICK_K, c, :], start=False, stop=c == PICK_CHUNKS - 1)
                        last.then_inc(onehot_used, 1)
                elif kind == "turn":
                    if n == 0:
                        pe.wait_ge(ident_ready, 2)
                    pe.wait_ge(raw_in[n % RAW_RING], 16 * FETCHES * (n // RAW_RING + 1))
                    if n >= 1:
                        pe.wait_ge(turn_out_a, n)
                    for k in range(FETCHES):
                        if k == FIRST_FETCHES and n >= 1:
                            pe.wait_ge(turn_out_b, n)
                        bank, at = (0, k) if k < FIRST_FETCHES else (1, k - FIRST_FETCHES)
                        last = nc.tensor.transpose(turn_ps[:, bank, 128 * at:128 * (at + 1)], raw[:, n % RAW_RING, k, :], ident[:, :])
                        if k == FIRST_FETCHES - 1:
                            last.then_inc(turned_a, 1)
                    last.then_inc(turned_b, 1)
                elif kind == "dots":
                    if n == 0:
                        pe.wait_ge(pad_zero, 1)
                        pe.wait_ge(pick_out, PICKS)
                    pe.wait_ge(turn_out_a, n + 1)
                    pe.wait_ge(turn_out_b, n + 1)
                    if n >= 2:
                        pe.wait_ge(dots_out_act, n - 1)
                        pe.wait_ge(dots_out_dve, n - 1)
                    for q in range(SETS):
                        at = n * GROUP + SET * q
                        bank = 2 * (n % 2) + q // 4
                        last = nc.tensor.matmul(dots_ps[:, bank, COLS * (q % 4):COLS * (q % 4 + 1)],
                                                emb[:, at:at + SET, :].rearrange("p s f -> p (s f)"),
                                                emb[:, at:at + SET, 0:FEATURES], start=True, stop=True)
                    last.then_inc(dotted, 1)
                elif kind == "layer1":
                    done = GROUPS_PER_TILE * (n + 1)
                    pe.wait_ge(dots_out_act, done)
                    pe.wait_ge(dots_out_dve, done)
                    if n == 0:
                        pe.wait_ge(w1_in, 16)
                        pe.wait_ge(dense_in, 16)
                    if n >= 1:
                        pe.wait_ge(h2_ready, n)
                        pe.wait_ge(y_ready, n)
                    for m in range(CHUNKS1):
                        for t in range(STEPS):
                            last = nc.tensor.matmul(acc_ps[:, m // 2, 128 * (m % 2):128 * (m % 2 + 1)],
                                                    w1_sb[:, t, 128 * m:128 * (m + 1)], dots[:, t, n * TILE:(n + 1) * TILE],
                                                    start=t == 0, stop=t == STEPS - 1)
                        if m == 1:
                            last.then_inc(layer1_a, 1)
                    last.then_inc(layer1_b, 1)
                elif kind == "layer2":
                    pe.wait_ge(h1_a, n + 1)
                    pe.wait_ge(h1_b, n + 1)
                    if n == 0:
                        pe.wait_ge(w23_in, 64)
                    for m in range(CHUNKS2):
                        for k in range(CHUNKS1):
                            last = nc.tensor.matmul(acc_ps[:, 0, 128 * m:128 * (m + 1)], w2_sb[:, k, 128 * m:128 * (m + 1)],
                                                    h1[:, k, :], start=k == 0, stop=k == CHUNKS1 - 1)
                    last.then_inc(layer2_done, 1)
                else:
                    pe.wait_ge(h2_ready, n + 1)
                    for k in range(CHUNKS2):
                        last = nc.tensor.matmul(acc_ps[0:1, 1, 0:TILE], w3_sb[:, k:k + 1], h2[:, k, :],
                                                start=k == 0, stop=k == CHUNKS2 - 1)
                    last.then_inc(layer3_done, 1)


def kernel(**inputs):
    import concourse.bacc as bacc
    from concourse import mybir
    from concourse.bass_utils import run_bass_kernel_spmd

    tables = [np.ascontiguousarray(inputs[f"tbl_{f}"]) for f in range(FEATURES)]
    ids = np.ascontiguousarray(inputs["ids"])
    fetch_ids = ids[:, FETCHED].reshape(GROUPS, GROUP, FETCHES, PER_FETCH).transpose(3, 1, 0, 2).reshape(128, -1)
    starts = np.concatenate([[0], np.cumsum([TABLE_ROWS[f] for f in FETCHED])[:-1]]).astype(np.int32)
    base = np.broadcast_to(starts.reshape(1, 1, FETCHES, PER_FETCH), (GROUPS, GROUP, FETCHES, PER_FETCH))
    pick_rows = np.arange(PICK_K * PICK_CHUNKS, dtype=np.float32).reshape(PICK_K, PICK_CHUNKS)
    pick_rows = np.concatenate([pick_rows, np.zeros((128 - PICK_K, PICK_CHUNKS), np.float32)])
    W1 = np.ascontiguousarray(inputs["W_top1"])
    w1 = np.zeros((4, QUAD, STEPS, HID1), W1.dtype)
    for j in range(1, FEATURES):
        for i in range(j):
            lo, hi = sorted((SLOTS[i], SLOTS[j]))
            w1[j // STEPS, i, j % STEPS] = W1[hi * (hi - 1) // 2 + lo]
    w1[3, 0:DENSE, STEPS - 1] = W1[FEATURES * (FEATURES - 1) // 2:]
    arrays = {
        "table": np.concatenate([tables[f] for f in FETCHED]),
        "fetch_ids": fetch_ids,
        "fetch_base": base.transpose(3, 1, 0, 2).reshape(128, -1),
        "pick_ids": ids[:, PICKED].T,
        **{f"pick_table{n}": tables[f] for n, f in enumerate(PICKED)},
        "pick_rows": pick_rows,
        "dense": inputs["dense_ctx"].T,
        "w1": w1.reshape(128, STEPS, HID1),
        "b1": inputs["b_top1"].reshape(CHUNKS1, 128).T,
        "w2": inputs["W_top2"],
        "b2": inputs["b_top2"].reshape(CHUNKS2, 128).T,
        "w3": inputs["W_top3"].reshape(CHUNKS2, 128).T,
    }
    arrays = {k: np.ascontiguousarray(a) for k, a in arrays.items()}
    nc = bacc.Bacc("TRN2", target_bir_lowering=False, num_devices=1)
    ap = {k: nc.dram_tensor(f"in_{k}", a.shape, mybir.dt.from_np(a.dtype), kind="ExternalInput").ap() for k, a in arrays.items()}
    y = nc.dram_tensor("out_y", (1, BATCH), mybir.dt.float32, kind="ExternalOutput").ap()
    build(nc, ap["table"], ap["fetch_ids"], ap["fetch_base"], ap["pick_ids"], [ap[f"pick_table{n}"] for n in range(PICKS)],
          ap["pick_rows"], ap["dense"], ap["w1"], ap["b1"], ap["w2"], ap["b2"], ap["w3"], y)
    r = run_bass_kernel_spmd(nc, [{f"in_{k}": a for k, a in arrays.items()}], core_ids=[0])
    return r.results[0]["out_y"].reshape(BATCH, 1)
```

```python
import numpy as np

TABLE_ROWS = [1250, 1250, 1000, 1000, 125000, 12500, 1000, 1000, 1250, 12500, 1000, 1000, 12500, 1250,
              12500, 1000, 12500, 12500, 1000, 1250, 1250, 1000, 12500, 1250, 12500, 1000, 1250]
FEATURES = len(TABLE_ROWS)
BATCH, EMBED, DENSE, HID1, HID2 = 512, 128, 16, 512, 256

PICKED_ROWS = 1000
PICKED = [f for f, rows in enumerate(TABLE_ROWS) if rows == PICKED_ROWS][:7]
FETCHED = [f for f in range(FEATURES) if f not in PICKED]
SLOTS = FETCHED + PICKED
PICKS = len(PICKED)

QUAD = 32
GROUP = 32
GROUPS = BATCH // GROUP
PER_FETCH = 128 // GROUP
FETCHES = len(FETCHED) // PER_FETCH
TILE = 128
TILES = BATCH // TILE
GROUPS_PER_TILE = TILE // GROUP
SET = 4
SETS = GROUP // SET

BLOCK = 9
BLOCKS = FEATURES // BLOCK
PLACES = 2 * BLOCK - 1
QUAD_PLACES = [(0, 5), (5, 8), (8, 13), (13, PLACES)]
STEPS = max(b - a for a, b in QUAD_PLACES)
FREE_QUADS = [c for c, (a, b) in enumerate(QUAD_PLACES) if b - a < STEPS]
DENSE_QUAD, DENSE_STEP = 3, STEPS - 1
WARM_UPS = 11
ORDER = """p0 p1 t0 p2 t1 p3 t2 p4 t3 p5 t4 p6 t5
           d0 d1 t6 d2 d3 t7 d4 a0 t8 d5 b0 t9 d6 c0 d7 t10 d8 a1 t11 d9 b1 t12 d10 c1
           d11 t13 d12 a2 t14 d13 t15 d14 d15 b2 c2 a3 b3 c3""".split()
PICK_K = 125
PICK_CHUNKS = PICKED_ROWS // PICK_K
CHUNKS1, CHUNKS2 = HID1 // 128, HID2 // 128
RAW_RING = 6
TABLE_RING = 3


def build(nc, table, fetch_ids, pick_ids, pick_tables, pick_rows, dense, w1, b1, w2, b2, w3, y):
    import concourse.bass as bass
    from concourse import mybir
    from contextlib import ExitStack

    F32, F32R, I32 = mybir.dt.float32, mybir.dt.float32r, mybir.dt.int32
    ALU, ACT = mybir.AluOpType, mybir.ActivationFunctionType

    ctx = ExitStack()
    with ctx:
        def sb(name, shape, dt=F32):
            return ctx.enter_context(nc.sbuf_tensor(name, shape, dt))

        def pb(name, shape):
            return ctx.enter_context(nc.psum_tensor(name, shape, F32))

        def sem(name):
            return ctx.enter_context(nc.semaphore(name))

        ids_sb = sb("ids_sb", [128, 2, GROUPS * FETCHES], I32)
        rows_sb = sb("rows_sb", [128, GROUPS * FETCHES], I32)
        raw = sb("raw", [128, RAW_RING, FETCHES, EMBED])
        pick_ids_sb = sb("pick_ids_sb", [128, PICKS, BATCH], I32)
        pick_rows_sb = sb("pick_rows_sb", [128, PICK_CHUNKS])
        tab = sb("tab", [128, TABLE_RING, PICK_CHUNKS * EMBED])
        tab_hi = sb("tab_hi", [128, TABLE_RING, PICK_CHUNKS * EMBED], F32R)
        tab_lo = sb("tab_lo", [128, TABLE_RING, PICK_CHUNKS * EMBED], F32R)
        onehot = sb("onehot", [128, PICK_CHUNKS, BATCH], F32R)
        emb = sb("emb", [128, BATCH, QUAD])
        dots = sb("dots", [128, STEPS, BATCH])
        w1_sb = sb("w1_sb", [128, STEPS, HID1])
        w2_sb = sb("w2_sb", [128, CHUNKS1, HID2])
        w3_sb = sb("w3_sb", [128, CHUNKS2])
        b1_sb = sb("b1_sb", [128, CHUNKS1])
        b2_sb = sb("b2_sb", [128, CHUNKS2])
        ident = sb("ident", [128, 128])
        h1 = sb("h1", [128, CHUNKS1, TILE])
        h2 = sb("h2", [128, CHUNKS2, TILE])
        y_sb = sb("y_sb", [1, BATCH])

        turn_ps = pb("turn_ps", [128, 2, 512])
        dots_ps = pb("dots_ps", [128, 4, 512])
        acc_ps = pb("acc_ps", [128, 2, 512])

        ids_in = sem("ids_in")
        rows_ready = sem("rows_ready")
        ident_ready = sem("ident_ready")
        raw_in = [sem(f"raw_in{r}") for r in range(RAW_RING)]
        pick_rows_in = sem("pick_rows_in")
        pick_ids_in = [sem(f"pick_ids_in{n}") for n in range(PICKS)]
        tab_in = [sem(f"tab_in{r}") for r in range(TABLE_RING)]
        hi_ready = sem("hi_ready")
        lo_ready = sem("lo_ready")
        onehot_ready = sem("onehot_ready")
        onehot_used = sem("onehot_used")
        pick_out = sem("pick_out")
        turned_a = sem("turned_a")
        turned_b = sem("turned_b")
        turn_out_a = sem("turn_out_a")
        turn_out_b = sem("turn_out_b")
        pad_zero = sem("pad_zero")
        free_zero = sem("free_zero")
        dense_in = sem("dense_in")
        w1_in = sem("w1_in")
        w23_in = sem("w23_in")
        dotted = sem("dotted")
        dots_out_act = sem("dots_out_act")
        dots_out_dve = sem("dots_out_dve")
        layer1_a = sem("layer1_a")
        layer1_b = sem("layer1_b")
        h1_a = sem("h1_a")
        h1_b = sem("h1_b")
        layer2_done = sem("layer2_done")
        h2_ready = sem("h2_ready")
        layer3_done = sem("layer3_done")
        y_ready = sem("y_ready")
        y_written = sem("y_written")

        FIRST_FETCHES = 3
        DOTS_OUTS = 2 * BLOCKS
        kinds = {"p": "pick", "t": "turn", "d": "dots", "a": "layer1", "b": "layer2", "c": "layer3"}
        order = [(kinds[x[0]], int(x[1:])) for x in ORDER]
        COLS = SET * FEATURES

        def turn_out(engine_copy, g, bank):
            a, b = (0, FIRST_FETCHES) if bank == 0 else (FIRST_FETCHES, FETCHES)
            src = turn_ps[:, bank, 0:(b - a) * 128].rearrange("p (f s) -> p f s", s=GROUP)
            dst = emb[:, g * GROUP:(g + 1) * GROUP, PER_FETCH * a:PER_FETCH * b].rearrange("p s f -> p f s")
            return engine_copy(dst, src)

        def dots_out(engine, engine_copy, g, samples, out):
            half = 2 * (g % 2)
            for turn, block in enumerate(reversed(range(BLOCKS))):
                rows = QUAD if block == BLOCKS - 1 else BLOCK * (block + 1)
                for at, s in enumerate(samples):
                    if turn >= 1:
                        engine.wait_ge(out, DOTS_OUTS * g + 2 * (turn - 1) + at + 1)
                    for c, (k0, k1) in enumerate(QUAD_PLACES):
                        j = FEATURES * s + (BLOCK * block + 1 + k0) % FEATURES
                        src = dots_ps[QUAD * s:QUAD * s + rows, half:half + 2, 0:4 * COLS].rearrange(
                            "p b (q x) -> p b q x", q=4)[:, :, :, j:j + k1 - k0]
                        dst = dots[QUAD * c:QUAD * c + rows, 0:k1 - k0, g * GROUP:(g + 1) * GROUP].rearrange(
                            "p t (b q s) -> p b q t s", b=2, q=4)[:, :, :, :, s]
                        last = engine_copy(dst, src)
                    last.then_inc(out, 1)

        def load_table(queue, n):
            rows = pick_tables[n].rearrange("(p c) d -> p (c d)", c=PICK_CHUNKS)
            queue.dma_start(tab[0:120, n % TABLE_RING, :], rows[0:120, :]).then_inc(tab_in[n % TABLE_RING], 16)
            queue.dma_start(tab[120:PICK_K, n % TABLE_RING, :], rows[120:PICK_K, :]).then_inc(tab_in[n % TABLE_RING], 16)

        block = ctx.enter_context(nc.Block())

        @block.sync
        def _(sp):
            sp.dma_start(ids_sb[:, :, :], fetch_ids.rearrange("i p n -> p i n")).then_inc(ids_in, 16)
            sp.dma_start(pick_rows_sb[:, :], pick_rows).then_inc(pick_rows_in, 16)
            for n in range(PICKS):
                sp.dma_start(pick_ids_sb[:, n, :], pick_ids[n:n + 1, :].broadcast_to([128, BATCH])).then_inc(pick_ids_in[n], 16)
                if n >= TABLE_RING:
                    sp.wait_ge(lo_ready, n - TABLE_RING + 1)
                    sp.wait_ge(hi_ready, n - TABLE_RING + 1)
                if n >= 1:
                    load_table(sp, n)
                if n == 2:
                    sp.dma_start(w1_sb[:, :, :], w1).then_inc(w1_in, 16)
            sp.dma_start(w2_sb[:, :, :], w2.rearrange("(c p) n -> p c n", p=128)).then_inc(w23_in, 16)
            sp.dma_start(w3_sb[:, :], w3).then_inc(w23_in, 16)
            sp.dma_start(b1_sb[:, :], b1).then_inc(w23_in, 16)
            sp.dma_start(b2_sb[:, :], b2).then_inc(w23_in, 16)
            sp.wait_ge(free_zero, len(FREE_QUADS))
            sp.dma_start(dots[DENSE_QUAD * QUAD:DENSE_QUAD * QUAD + DENSE, DENSE_STEP, :], dense).then_inc(dense_in, 16)
            sp.wait_ge(y_ready, TILES)
            sp.dma_start(y, y_sb[:, :]).then_inc(y_written, 16)
            sp.wait_ge(y_written, 16)

        @block.gpsimd
        def _(pool):
            nc.gpsimd.memset(ident[:, :], 0.0).then_inc(ident_ready, 1)
            pool.wait_ge(ident_ready, 1)
            nc.gpsimd.affine_select(out=ident[:, :], in_=ident[:, :], compare_op=ALU.not_equal, fill=1.0, base=0,
                                    pattern=[[-1, 128]], channel_multiplier=1).then_inc(ident_ready, 1)
            pool.wait_ge(ident_ready, 2)
            for i, c in enumerate(FREE_QUADS):
                if i >= 1:
                    pool.wait_ge(free_zero, i)
                k0, k1 = QUAD_PLACES[c]
                nc.gpsimd.memset(dots[QUAD * c:QUAD * (c + 1), k1 - k0:STEPS, :], 0.0).then_inc(free_zero, 1)
            pool.wait_ge(rows_ready, 1)
            for g in range(GROUPS):
                if g >= RAW_RING:
                    pool.wait_ge(turned_b, g - RAW_RING + 1)
                for k in range(FETCHES):
                    at = g * FETCHES + k
                    pool.indirect_dma_start(raw[:, g % RAW_RING, k, :], None, table,
                                            bass.IndirectOffsetOnAxis(rows_sb[:, at:at + 1], 0)).then_inc(
                                                raw_in[g % RAW_RING], 16)

        @block.vector
        def _(dve):
            nc.vector.memset(emb[:, :, FEATURES:QUAD], 0.0).then_inc(pad_zero, 1)
            dve.wait_ge(ids_in, 16)
            nc.vector.tensor_tensor(rows_sb[:, :], ids_sb[:, 0, :], ids_sb[:, 1, :], ALU.add).then_inc(rows_ready, 1)
            dve.wait_ge(pick_rows_in, 16)
            for kind, n in order:
                if kind == "pick":
                    dve.wait_ge(pick_ids_in[n], 16)
                    for c in range(PICK_CHUNKS):
                        if n >= 1:
                            dve.wait_ge(onehot_used, (n - 1) * PICK_CHUNKS + c + 1)
                        nc.vector.tensor_scalar(onehot[0:PICK_K, c, :], pick_ids_sb[0:PICK_K, n, :],
                                                pick_rows_sb[0:PICK_K, c:c + 1], None, ALU.is_equal).then_inc(onehot_ready, 1)
                        if c == (PICK_CHUNKS - 1 if n == 0 else 0):
                            dve.wait_ge(hi_ready, n + 1)
                            dve.wait_ge(tab_in[n % TABLE_RING], 32 * (n // TABLE_RING + 1))
                            if n >= TABLE_RING:
                                dve.wait_ge(onehot_used, PICK_CHUNKS * (n - TABLE_RING + 1))
                            nc.vector.tensor_tensor(tab_lo[0:PICK_K, n % TABLE_RING, :], tab[0:PICK_K, n % TABLE_RING, :],
                                                    tab_hi[0:PICK_K, n % TABLE_RING, :].bitcast(F32), ALU.subtract).then_inc(lo_ready, 1)
                elif kind == "dots":
                    dve.wait_ge(dotted, n + 1)
                    dots_out(dve, nc.vector.tensor_copy, n, (2, 3), dots_out_dve)
                elif kind == "layer1":
                    if n == 0:
                        dve.wait_ge(w23_in, 64)
                    if n >= 1:
                        dve.wait_ge(layer2_done, n)
                    dve.wait_ge(layer1_b, n + 1)
                    for m in (2, 3):
                        last = nc.vector.tensor_scalar(h1[:, m, :], acc_ps[:, 1, 128 * (m - 2):128 * (m - 1)],
                                                       b1_sb[:, m:m + 1], 0.0, ALU.add, ALU.max)
                    last.then_inc(h1_b, 1)

        @block.scalar
        def _(act):
            load_table(act, 0)

            def high_half(n):
                act.wait_ge(tab_in[n % TABLE_RING], 32 * (n // TABLE_RING + 1))
                if n >= TABLE_RING:
                    act.wait_ge(onehot_used, PICK_CHUNKS * (n - TABLE_RING + 1))
                nc.scalar.copy(tab_hi[0:PICK_K, n % TABLE_RING, :], tab[0:PICK_K, n % TABLE_RING, :]).then_inc(hi_ready, 1)

            for kind, n in order:
                if kind == "pick":
                    if n == 0:
                        high_half(0)
                    if n + 1 < PICKS:
                        high_half(n + 1)
                    if n >= 1:
                        act.wait_ge(onehot_used, PICK_CHUNKS * n)
                        nc.scalar.copy(emb[:, :, len(FETCHED) + n - 1], acc_ps[:, (n - 1) % 2, :]).then_inc(pick_out, 1)
                elif kind == "turn":
                    if n == PICKS - 2:
                        act.wait_ge(onehot_used, PICK_CHUNKS * PICKS)
                        nc.scalar.copy(emb[:, :, FEATURES - 1], acc_ps[:, (PICKS - 1) % 2, :]).then_inc(pick_out, 1)
                    act.wait_ge(turned_a, n + 1)
                    turn_out(nc.scalar.copy, n, 0).then_inc(turn_out_a, 1)
                    act.wait_ge(turned_b, n + 1)
                    turn_out(nc.scalar.copy, n, 1).then_inc(turn_out_b, 1)
                elif kind == "dots":
                    act.wait_ge(dotted, n + 1)
                    dots_out(act, nc.scalar.copy, n, (0, 1), dots_out_act)
                elif kind == "layer1":
                    if n == 0:
                        act.wait_ge(w23_in, 64)
                    if n >= 1:
                        act.wait_ge(layer2_done, n)
                    act.wait_ge(layer1_a, n + 1)
                    for m in (0, 1):
                        last = nc.scalar.activation(h1[:, m, :], acc_ps[:, 0, 128 * m:128 * (m + 1)], ACT.Relu,
                                                    bias=b1_sb[:, m:m + 1])
                    last.then_inc(h1_a, 1)
                elif kind == "layer2":
                    if n >= 1:
                        act.wait_ge(layer3_done, n)
                    act.wait_ge(layer2_done, n + 1)
                    for m in range(CHUNKS2):
                        last = nc.scalar.activation(h2[:, m, :], acc_ps[:, 0, 128 * m:128 * (m + 1)], ACT.Relu,
                                                    bias=b2_sb[:, m:m + 1])
                    last.then_inc(h2_ready, 1)
                else:
                    act.wait_ge(layer3_done, n + 1)
                    nc.scalar.copy(y_sb[:, n * TILE:(n + 1) * TILE], acc_ps[0:1, 1, 0:TILE]).then_inc(y_ready, 1)

        @block.tensor
        def _(pe):
            pe.wait_ge(ident_ready, 2)
            for _ in range(WARM_UPS):
                nc.tensor.matmul(turn_ps[:, 1, 0:128], ident[:, :], ident[:, :], start=True, stop=True)
            for kind, n in order:
                if kind == "pick":
                    pe.wait_ge(hi_ready, n + 1)
                    if n >= 1:
                        pe.wait_ge(lo_ready, n + 1)
                    if n >= 2:
                        pe.wait_ge(pick_out, n - 1)
                    passes = [[(tab_hi, c)] for c in range(PICK_CHUNKS)] + [[(tab_lo, c)] for c in range(PICK_CHUNKS)]
                    if n >= 1:
                        passes = [[(tab_hi, c), (tab_lo, c)] for c in range(PICK_CHUNKS)]
                    for products in passes:
                        for part, c in products:
                            if part is tab_hi:
                                pe.wait_ge(onehot_ready, n * PICK_CHUNKS + c + 1)
                            elif n == 0 and c == 0:
                                pe.wait_ge(lo_ready, 1)
                            last = nc.tensor.matmul(acc_ps[:, n % 2, :], part[0:PICK_K, n % TABLE_RING, EMBED * c:EMBED * (c + 1)],
                                                    onehot[0:PICK_K, c, :], start=part is tab_hi and c == 0,
                                                    stop=part is tab_lo and c == PICK_CHUNKS - 1)
                        if part is tab_lo:
                            last.then_inc(onehot_used, 1)
                elif kind == "turn":
                    pe.wait_ge(raw_in[n % RAW_RING], 16 * FETCHES * (n // RAW_RING + 1))
                    if n >= 1:
                        pe.wait_ge(turn_out_a, n)
                    for k in range(FETCHES):
                        if k == FIRST_FETCHES and n >= 1:
                            pe.wait_ge(turn_out_b, n)
                        bank, at = (0, k) if k < FIRST_FETCHES else (1, k - FIRST_FETCHES)
                        last = nc.tensor.transpose(turn_ps[:, bank, 128 * at:128 * (at + 1)], raw[:, n % RAW_RING, k, :], ident[:, :])
                        if k == FIRST_FETCHES - 1:
                            last.then_inc(turned_a, 1)
                    last.then_inc(turned_b, 1)
                elif kind == "dots":
                    if n == 0:
                        pe.wait_ge(pad_zero, 1)
                        pe.wait_ge(pick_out, PICKS)
                    pe.wait_ge(turn_out_a, n + 1)
                    pe.wait_ge(turn_out_b, n + 1)
                    if n >= 2:
                        pe.wait_ge(dots_out_act, DOTS_OUTS * (n - 1))
                        pe.wait_ge(dots_out_dve, DOTS_OUTS * (n - 1))
                    for q in range(SETS):
                        at = n * GROUP + SET * q
                        bank = 2 * (n % 2) + q // 4
                        last = nc.tensor.matmul(dots_ps[:, bank, COLS * (q % 4):COLS * (q % 4 + 1)],
                                                emb[:, at:at + SET, :].rearrange("p s f -> p (s f)"),
                                                emb[:, at:at + SET, 0:FEATURES], start=True, stop=True)
                    last.then_inc(dotted, 1)
                elif kind == "layer1":
                    done = DOTS_OUTS * GROUPS_PER_TILE * (n + 1)
                    pe.wait_ge(dots_out_act, done)
                    pe.wait_ge(dots_out_dve, done)
                    if n == 0:
                        pe.wait_ge(w1_in, 16)
                        pe.wait_ge(dense_in, 16)
                    if n >= 1:
                        pe.wait_ge(h2_ready, n)
                        pe.wait_ge(y_ready, n)
                    for m in range(CHUNKS1):
                        for t in range(STEPS):
                            last = nc.tensor.matmul(acc_ps[:, m // 2, 128 * (m % 2):128 * (m % 2 + 1)],
                                                    w1_sb[:, t, 128 * m:128 * (m + 1)], dots[:, t, n * TILE:(n + 1) * TILE],
                                                    start=t == 0, stop=t == STEPS - 1)
                        if m == 1:
                            last.then_inc(layer1_a, 1)
                    last.then_inc(layer1_b, 1)
                elif kind == "layer2":
                    pe.wait_ge(h1_a, n + 1)
                    pe.wait_ge(h1_b, n + 1)
                    if n == 0:
                        pe.wait_ge(w23_in, 64)
                    for m in range(CHUNKS2):
                        for k in range(CHUNKS1):
                            last = nc.tensor.matmul(acc_ps[:, 0, 128 * m:128 * (m + 1)], w2_sb[:, k, 128 * m:128 * (m + 1)],
                                                    h1[:, k, :], start=k == 0, stop=k == CHUNKS1 - 1)
                    last.then_inc(layer2_done, 1)
                else:
                    pe.wait_ge(h2_ready, n + 1)
                    for k in range(CHUNKS2):
                        last = nc.tensor.matmul(acc_ps[0:1, 1, 0:TILE], w3_sb[:, k:k + 1], h2[:, k, :],
                                                start=k == 0, stop=k == CHUNKS2 - 1)
                    last.then_inc(layer3_done, 1)


def kernel(**inputs):
    import concourse.bacc as bacc
    from concourse import mybir
    from concourse.bass_utils import run_bass_kernel_spmd

    tables = [np.ascontiguousarray(inputs[f"tbl_{f}"]) for f in range(FEATURES)]
    ids = np.ascontiguousarray(inputs["ids"])
    fetch_ids = ids[:, FETCHED].reshape(GROUPS, GROUP, FETCHES, PER_FETCH).transpose(3, 1, 0, 2).reshape(128, -1)
    starts = np.concatenate([[0], np.cumsum([TABLE_ROWS[f] for f in FETCHED])[:-1]]).astype(np.int32)
    base = np.broadcast_to(starts.reshape(1, 1, FETCHES, PER_FETCH), (GROUPS, GROUP, FETCHES, PER_FETCH))
    pick_rows = np.arange(PICK_K * PICK_CHUNKS, dtype=np.float32).reshape(PICK_K, PICK_CHUNKS)
    pick_rows = np.concatenate([pick_rows, np.zeros((128 - PICK_K, PICK_CHUNKS), np.float32)])
    W1 = np.ascontiguousarray(inputs["W_top1"])
    w1 = np.zeros((4, QUAD, STEPS, HID1), W1.dtype)
    for i in range(FEATURES):
        for c, (k0, k1) in enumerate(QUAD_PLACES):
            for k in range(k0, k1):
                j = (i // BLOCK * BLOCK + 1 + k) % FEATURES
                if j // BLOCK != i // BLOCK or j > i:
                    lo, hi = sorted((SLOTS[i], SLOTS[j]))
                    w1[c, i, k - k0] = W1[hi * (hi - 1) // 2 + lo]
    w1[DENSE_QUAD, 0:DENSE, DENSE_STEP] = W1[FEATURES * (FEATURES - 1) // 2:]
    arrays = {
        "table": np.concatenate([tables[f] for f in FETCHED]),
        "fetch_ids": np.stack([fetch_ids, base.transpose(3, 1, 0, 2).reshape(128, -1)]),
        "pick_ids": ids[:, PICKED].T,
        **{f"pick_table{n}": tables[f] for n, f in enumerate(PICKED)},
        "pick_rows": pick_rows,
        "dense": inputs["dense_ctx"].T,
        "w1": w1.reshape(128, STEPS, HID1),
        "b1": inputs["b_top1"].reshape(CHUNKS1, 128).T,
        "w2": inputs["W_top2"],
        "b2": inputs["b_top2"].reshape(CHUNKS2, 128).T,
        "w3": inputs["W_top3"].reshape(CHUNKS2, 128).T,
    }
    arrays = {k: np.ascontiguousarray(a) for k, a in arrays.items()}
    nc = bacc.Bacc("TRN2", target_bir_lowering=False, num_devices=1)
    ap = {k: nc.dram_tensor(f"in_{k}", a.shape, mybir.dt.from_np(a.dtype), kind="ExternalInput").ap() for k, a in arrays.items()}
    y = nc.dram_tensor("out_y", (1, BATCH), mybir.dt.float32, kind="ExternalOutput").ap()
    build(nc, ap["table"], ap["fetch_ids"], ap["pick_ids"], [ap[f"pick_table{n}"] for n in range(PICKS)],
          ap["pick_rows"], ap["dense"], ap["w1"], ap["b1"], ap["w2"], ap["b2"], ap["w3"], y)
    r = run_bass_kernel_spmd(nc, [{f"in_{k}": a for k, a in arrays.items()}], core_ids=[0])
    return r.results[0]["out_y"].reshape(BATCH, 1)
```

```python
import numpy as np

TABLE_ROWS = [1250, 1250, 1000, 1000, 125000, 12500, 1000, 1000, 1250, 12500, 1000, 1000, 12500, 1250,
              12500, 1000, 12500, 12500, 1000, 1250, 1250, 1000, 12500, 1250, 12500, 1000, 1250]
FEATURES = len(TABLE_ROWS)
BATCH, EMBED, DENSE, HID1, HID2 = 512, 128, 16, 512, 256

PICKED_ROWS = 1000
PICKED = [f for f, rows in enumerate(TABLE_ROWS) if rows == PICKED_ROWS][:7]
FETCHED = [f for f in range(FEATURES) if f not in PICKED]
SLOTS = FETCHED + PICKED
PICKS = len(PICKED)

QUAD = 32
GROUP = 32
GROUPS = BATCH // GROUP
PER_FETCH = 128 // GROUP
FETCHES = len(FETCHED) // PER_FETCH
TILE = 128
TILES = BATCH // TILE
GROUPS_PER_TILE = TILE // GROUP
SET = 4
SETS = GROUP // SET

BLOCK = 9
BLOCKS = FEATURES // BLOCK
PLACES = 2 * BLOCK - 1
QUAD_PLACES = [(0, 5), (5, 8), (8, 13), (13, PLACES)]
STEPS = max(b - a for a, b in QUAD_PLACES)
FREE_QUADS = [c for c, (a, b) in enumerate(QUAD_PLACES) if b - a < STEPS]
DENSE_QUAD, DENSE_STEP = 3, STEPS - 1
PE_ORDER = """p0 p1 p2 t0 p3 t1 p4 t2 p5 t3 p6 t4 d0 t5 d1 d2 d3 t6 d4 u0 d5 t7 d6 t8 v0 d7 d8 t9 x0 d9 y0
             t10 u1 v1 t11 d10 d11 x1 t12 y1 d12 u2 t13 v2 d13 t14 x2 d14 t15 y2 d15 z3""".split()
OUT_ORDER = """p0 p1 p2 p3 t0 p4 t1 p5 t2 p6 t3 q6 t4 d0 d1 d2 t5 d3 t6 d4 t7 d5 u0 t8 d6 v0 d7 t9 x0 y0 d8 d9
             t10 u1 t11 v1 d10 x1 t12 d11 y1 t13 u2 d12 v2 t14 d13 x2 t15 d14 d15 y2 z3""".split()

TURNS_AMONG_PICKS = 6
PICK_K = 125
PICK_CHUNKS = PICKED_ROWS // PICK_K
DVE_CHUNKS = PICK_CHUNKS - 1
CHUNKS1, CHUNKS2 = HID1 // 128, HID2 // 128
RAW_RING = 6
TABLE_RING = 3
ONEHOT_RING = 12


def build(nc, table, fetch_ids, pick_ids, pick_tables, dense, w1, b1, w2, b2, w3, y):
    import concourse.bass as bass
    from concourse import mybir
    from contextlib import ExitStack

    F32, F32R, I32 = mybir.dt.float32, mybir.dt.float32r, mybir.dt.int32
    ALU, ACT = mybir.AluOpType, mybir.ActivationFunctionType

    ctx = ExitStack()
    with ctx:
        def sb(name, shape, dt=F32):
            return ctx.enter_context(nc.sbuf_tensor(name, shape, dt))

        def pb(name, shape):
            return ctx.enter_context(nc.psum_tensor(name, shape, F32))

        def sem(name):
            return ctx.enter_context(nc.semaphore(name))

        ids_sb = sb("ids_sb", [128, 2 * GROUPS * FETCHES + PICK_CHUNKS], I32)
        rows_sb = sb("rows_sb", [128, GROUPS * FETCHES], I32)
        raw = sb("raw", [128, RAW_RING, FETCHES, EMBED])
        pick_ids_sb = sb("pick_ids_sb", [128, PICKS, BATCH], I32)
        pick_rows_sb = sb("pick_rows_sb", [128, PICK_CHUNKS])
        tab = sb("tab", [128, TABLE_RING, PICK_CHUNKS * EMBED])
        tab_hi = sb("tab_hi", [128, TABLE_RING, PICK_CHUNKS * EMBED], F32R)
        tab_lo = sb("tab_lo", [128, TABLE_RING, PICK_CHUNKS * EMBED], F32R)
        onehot = sb("onehot", [128, ONEHOT_RING, BATCH], F32R)
        distance = sb("distance", [128, BATCH])
        emb = sb("emb", [128, BATCH, QUAD])
        dots = sb("dots", [128, STEPS, BATCH])
        w1_sb = sb("w1_sb", [128, STEPS, HID1])
        w2_sb = sb("w2_sb", [128, CHUNKS1, HID2])
        w3_sb = sb("w3_sb", [128, CHUNKS2])
        b1_sb = sb("b1_sb", [128, CHUNKS1])
        b2_sb = sb("b2_sb", [128, CHUNKS2])
        ident = sb("ident", [128, 128])
        zero = sb("zero", [128, 1, 1])
        h1 = sb("h1", [128, CHUNKS1, TILE])
        h2 = sb("h2", [128, CHUNKS2, TILE])
        y_sb = sb("y_sb", [1, BATCH])

        turn_ps = pb("turn_ps", [128, 2, 512])
        dots_ps = pb("dots_ps", [128, 4, 512])
        acc_ps = pb("acc_ps", [128, 2, 512])

        ids_in = sem("ids_in")
        rows_ready = sem("rows_ready")
        zero_ready = sem("zero_ready")
        ident_ready = sem("ident_ready")
        last_raw_in = sem("last_raw_in")
        raw_in = [sem(f"raw_in{r}") for r in range(RAW_RING)]
        pick_rows_ready = sem("pick_rows_ready")
        pick_ids_in = [sem(f"pick_ids_in{n}") for n in range(PICKS)]
        tab_in = [sem(f"tab_in{r}") for r in range(TABLE_RING)]
        hi_ready = sem("hi_ready")
        lo_ready = sem("lo_ready")
        onehot_ready = sem("onehot_ready")
        distance_ready = sem("distance_ready")
        last_onehot_ready = sem("last_onehot_ready")
        onehot_used = sem("onehot_used")
        pick_out = sem("pick_out")
        turned_a = sem("turned_a")
        turned_b = sem("turned_b")
        turn_out_a = sem("turn_out_a")
        turn_out_b = sem("turn_out_b")
        pad_zero = sem("pad_zero")
        free_zero = sem("free_zero")
        dense_in = sem("dense_in")
        w1_in = sem("w1_in")
        w23_in = sem("w23_in")
        dotted = sem("dotted")
        dots_out_act = sem("dots_out_act")
        dots_out_dve = sem("dots_out_dve")
        layer1_a = sem("layer1_a")
        layer1_b = sem("layer1_b")
        h1_a = sem("h1_a")
        h1_b = sem("h1_b")
        layer2_a = sem("layer2_a")
        layer2_b = sem("layer2_b")
        h2_a = sem("h2_a")
        h2_b = sem("h2_b")
        layer3_done = sem("layer3_done")
        y_ready = sem("y_ready")
        y_written = sem("y_written")

        FIRST_FETCHES = 3
        DOTS_OUTS = 2 * BLOCKS
        kinds = {"p": "pick", "q": "last_pick", "t": "turn", "d": "dots", "u": "layer1_first", "v": "layer1_second",
                 "x": "layer2", "y": "layer3", "z": "last_tile"}
        pe_order, out_order = ([(kinds[x[0]], int(x[1:])) for x in order] for order in (PE_ORDER, OUT_ORDER))
        COLS = SET * FEATURES

        def last_h1_ps(m):
            return (acc_ps, turn_ps)[m // 2][:, m % 2, 0:TILE]

        def turn_out(engine_copy, g, bank):
            a, b = (0, FIRST_FETCHES) if bank == 0 else (FIRST_FETCHES, FETCHES)
            src = turn_ps[:, bank, 0:(b - a) * 128].rearrange("p (f s) -> p f s", s=GROUP)
            dst = emb[:, g * GROUP:(g + 1) * GROUP, PER_FETCH * a:PER_FETCH * b].rearrange("p s f -> p f s")
            return engine_copy(dst, src)

        def dots_out(engine, engine_copy, g, samples, out):
            half = 2 * (g % 2)
            for turn, block in enumerate(reversed(range(BLOCKS))):
                rows = QUAD if block == BLOCKS - 1 else BLOCK * (block + 1)
                for at, s in enumerate(samples):
                    if turn >= 1:
                        engine.wait_ge(out, DOTS_OUTS * g + 2 * (turn - 1) + at + 1)
                    for c, (k0, k1) in enumerate(QUAD_PLACES):
                        j = FEATURES * s + (BLOCK * block + 1 + k0) % FEATURES
                        src = dots_ps[QUAD * s:QUAD * s + rows, half:half + 2, 0:4 * COLS].rearrange(
                            "p b (q x) -> p b q x", q=4)[:, :, :, j:j + k1 - k0]
                        dst = dots[QUAD * c:QUAD * c + rows, 0:k1 - k0, g * GROUP:(g + 1) * GROUP].rearrange(
                            "p t (b q s) -> p b q t s", b=2, q=4)[:, :, :, :, s]
                        last = engine_copy(dst, src)
                    last.then_inc(out, 1)

        def load_table(queue, n):
            rows = pick_tables[n].rearrange("(p c) d -> p (c d)", c=PICK_CHUNKS)
            queue.dma_start(tab[0:120, n % TABLE_RING, :], rows[0:120, :]).then_inc(tab_in[n % TABLE_RING], 16)
            queue.dma_start(tab[120:PICK_K, n % TABLE_RING, :], rows[120:PICK_K, :]).then_inc(tab_in[n % TABLE_RING], 16)

        block = ctx.enter_context(nc.Block())

        @block.sync
        def _(sp):
            sp.dma_start(ids_sb[:, :], fetch_ids).then_inc(ids_in, 16)
            for n in range(PICKS):
                sp.dma_start(pick_ids_sb[:, n, :], pick_ids[n:n + 1, :].broadcast_to([128, BATCH])).then_inc(pick_ids_in[n], 16)
                if n >= TABLE_RING:
                    sp.wait_ge(lo_ready, n - TABLE_RING + 1)
                    sp.wait_ge(hi_ready, n - TABLE_RING + 1)
                load_table(sp, n)
                if n == PICKS - 1:
                    sp.dma_start(w1_sb[:, :, :], w1).then_inc(w1_in, 16)
            sp.dma_start(w2_sb[:, :, :], w2.rearrange("(c p) n -> p c n", p=128)).then_inc(w23_in, 16)
            sp.dma_start(w3_sb[:, :], w3).then_inc(w23_in, 16)
            sp.dma_start(b1_sb[:, :], b1).then_inc(w23_in, 16)
            sp.dma_start(b2_sb[:, :], b2).then_inc(w23_in, 16)
            sp.wait_ge(free_zero, len(FREE_QUADS))
            sp.dma_start(dots[DENSE_QUAD * QUAD:DENSE_QUAD * QUAD + DENSE, DENSE_STEP, :], dense).then_inc(dense_in, 16)
            sp.wait_ge(y_ready, TILES)
            sp.dma_start(y, y_sb[:, :]).then_inc(y_written, 16)
            sp.wait_ge(y_written, 16)

        @block.gpsimd
        def _(pool):
            nc.gpsimd.memset(zero[:, :, :], 0.0).then_inc(zero_ready, 1)
            pool.wait_ge(zero_ready, 1)
            nc.gpsimd.memset(ident[:, :], 0.0).then_inc(ident_ready, 1)
            pool.wait_ge(ident_ready, 1)
            nc.gpsimd.affine_select(out=ident[:, :], in_=ident[:, :], compare_op=ALU.not_equal, fill=1.0, base=0,
                                    pattern=[[-1, 128]], channel_multiplier=1).then_inc(ident_ready, 1)
            pool.wait_ge(ident_ready, 2)
            for i, c in enumerate(FREE_QUADS):
                if i >= 1:
                    pool.wait_ge(free_zero, i)
                k0, k1 = QUAD_PLACES[c]
                nc.gpsimd.memset(dots[QUAD * c:QUAD * (c + 1), k1 - k0:STEPS, :], 0.0).then_inc(free_zero, 1)
            pool.wait_ge(rows_ready, 1)
            for g in range(GROUPS):
                if g >= RAW_RING:
                    pool.wait_ge(turned_b, g - RAW_RING + 1)
                for k in range(FETCHES):
                    at = g * FETCHES + k
                    pool.indirect_dma_start(raw[:, g % RAW_RING, k, :], None, table,
                                            bass.IndirectOffsetOnAxis(rows_sb[:, at:at + 1], 0)).then_inc(
                                                last_raw_in if at == GROUPS * FETCHES - 1 else raw_in[g % RAW_RING], 16)

        @block.vector
        def _(dve):
            def dve_relu(dst, src, bias):
                return nc.vector.tensor_scalar(dst, src, bias, 0.0, ALU.add, ALU.max)

            def low_half(n):
                dve.wait_ge(hi_ready, n + 1)
                dve.wait_ge(tab_in[n % TABLE_RING], 32 * (n // TABLE_RING + 1))
                if n >= TABLE_RING:
                    dve.wait_ge(onehot_used, PICK_CHUNKS * (n - TABLE_RING + 1))
                nc.vector.tensor_tensor(tab_lo[0:PICK_K, n % TABLE_RING, :], tab[0:PICK_K, n % TABLE_RING, :],
                                        tab_hi[0:PICK_K, n % TABLE_RING, :].bitcast(F32), ALU.subtract).then_inc(lo_ready, 1)

            dve.wait_ge(ids_in, 16)
            fetched = GROUPS * FETCHES
            nc.vector.tensor_tensor(rows_sb[:, :], ids_sb[:, 0:fetched], ids_sb[:, fetched:2 * fetched], ALU.add).then_inc(rows_ready, 1)
            nc.vector.tensor_copy(pick_rows_sb[:, :], ids_sb[:, 2 * fetched:2 * fetched + PICK_CHUNKS]).then_inc(pick_rows_ready, 1)
            dve.wait_ge(pick_rows_ready, 1)
            for kind, n in out_order:
                if kind == "pick":
                    dve.wait_ge(pick_ids_in[n], 16)
                    for c in range(DVE_CHUNKS):
                        if n >= 1 and c == 1:
                            low_half(n)
                        at = n * PICK_CHUNKS + c
                        if at >= ONEHOT_RING:
                            dve.wait_ge(onehot_used, at - ONEHOT_RING + 1)
                        nc.vector.tensor_scalar(onehot[0:PICK_K, at % ONEHOT_RING, :], pick_ids_sb[0:PICK_K, n, :],
                                                pick_rows_sb[0:PICK_K, c:c + 1], None, ALU.is_equal).then_inc(onehot_ready, 1)
                    if n == 0:
                        low_half(n)
                elif kind == "turn" and n >= TURNS_AMONG_PICKS:
                    dve.wait_ge(turned_b, n + 1)
                    turn_out(nc.vector.tensor_copy, n, 1).then_inc(turn_out_b, 1)
                elif kind == "dots":
                    dve.wait_ge(dotted, n + 1)
                    dots_out(dve, nc.vector.tensor_copy, n, (2, 3), dots_out_dve)
                elif kind == "layer1_second":
                    if n == 0:
                        dve.wait_ge(w23_in, 64)
                    if n >= 1:
                        dve.wait_ge(layer2_b, n)
                    dve.wait_ge(layer1_b, n + 1)
                    for m in (2, 3):
                        last = dve_relu(h1[:, m, :], acc_ps[:, 1, 128 * (m - 2):128 * (m - 1)], b1_sb[:, m:m + 1])
                    last.then_inc(h1_b, 1)
                elif kind == "layer2":
                    if n >= 1:
                        dve.wait_ge(layer3_done, n)
                    dve.wait_ge(layer2_b, n + 1)
                    dve_relu(h2[:, 1, :], acc_ps[:, 1, 0:TILE], b2_sb[:, 1:2]).then_inc(h2_b, 1)
                elif kind == "last_tile":
                    dve.wait_ge(layer2_b, n)
                    for i, m in enumerate((1, 3)):
                        dve.wait_ge(layer1_b, n + 1 + i)
                        dve_relu(h1[:, m, :], last_h1_ps(m), b1_sb[:, m:m + 1]).then_inc(h1_b, 1)
                    dve.wait_ge(layer3_done, n)
                    dve.wait_ge(layer2_b, n + 1)
                    dve_relu(h2[:, 1, :], dots_ps[:, 1, 0:TILE], b2_sb[:, 1:2]).then_inc(h2_b, 1)

        @block.scalar
        def _(act):
            def act_relu(dst, src, bias):
                return nc.scalar.activation(dst, src, ACT.Relu, bias=bias)

            def y_out_of_psum(n):
                act.wait_ge(layer3_done, n + 1)
                nc.scalar.copy(y_sb[:, n * TILE:(n + 1) * TILE], acc_ps[0:1, 0, 0:TILE]).then_inc(y_ready, 1)

            def high_half(n):
                act.wait_ge(tab_in[n % TABLE_RING], 32 * (n // TABLE_RING + 1))
                if n >= TABLE_RING:
                    act.wait_ge(onehot_used, PICK_CHUNKS * (n - TABLE_RING + 1))
                nc.scalar.copy(tab_hi[0:PICK_K, n % TABLE_RING, :], tab[0:PICK_K, n % TABLE_RING, :]).then_inc(hi_ready, 1)

            def id_distance(n):
                act.wait_ge(pick_ids_in[n], 16)
                if n >= 1:
                    act.wait_ge(last_onehot_ready, n)
                nc.scalar.activation(distance[0:PICK_K, :], pick_ids_sb[0:PICK_K, n, :], ACT.Abs, scale=-1.0,
                                     bias=pick_rows_sb[0:PICK_K, DVE_CHUNKS:PICK_CHUNKS]).then_inc(distance_ready, 1)

            def last_onehot(n):
                at = n * PICK_CHUNKS + DVE_CHUNKS
                if at >= ONEHOT_RING:
                    act.wait_ge(onehot_used, at - ONEHOT_RING + 1)
                act.wait_ge(distance_ready, n + 1)
                nc.scalar.activation(onehot[0:PICK_K, at % ONEHOT_RING, :], distance[0:PICK_K, :], ACT.Relu, scale=-1.0,
                                     bias=1.0).then_inc(last_onehot_ready, 1)

            def pick_out_of_psum(n):
                act.wait_ge(onehot_used, PICK_CHUNKS * (n + 1))
                nc.scalar.copy(emb[:, :, len(FETCHED) + n], acc_ps[:, n % 2, :]).then_inc(pick_out, 1)

            act.wait_ge(zero_ready, 1)
            nc.scalar.copy(emb[:, :, FEATURES:QUAD], zero.broadcast_to([128, BATCH, QUAD - FEATURES])).then_inc(pad_zero, 1)
            for kind, n in out_order:
                if kind == "pick":
                    if n == 0:
                        act.wait_ge(pick_rows_ready, 1)
                        id_distance(0)
                    if n >= 1 and n + 1 < PICKS:
                        high_half(n + 1)
                    last_onehot(n)
                    if n == 0:
                        high_half(0)
                        high_half(1)
                    else:
                        pick_out_of_psum(n - 1)
                    if n + 1 < PICKS:
                        id_distance(n + 1)
                elif kind == "last_pick":
                    pick_out_of_psum(n)
                elif kind == "turn":
                    act.wait_ge(turned_a, n + 1)
                    turn_out(nc.scalar.copy, n, 0).then_inc(turn_out_a, 1)
                    if n < TURNS_AMONG_PICKS:
                        act.wait_ge(turned_b, n + 1)
                        turn_out(nc.scalar.copy, n, 1).then_inc(turn_out_b, 1)
                elif kind == "dots":
                    act.wait_ge(dotted, n + 1)
                    dots_out(act, nc.scalar.copy, n, (0, 1), dots_out_act)
                elif kind == "layer1_first":
                    if n == 0:
                        act.wait_ge(w23_in, 64)
                    if n >= 1:
                        act.wait_ge(layer2_b, n)
                    act.wait_ge(layer1_a, n + 1)
                    for m in (0, 1):
                        last = act_relu(h1[:, m, :], acc_ps[:, 0, 128 * m:128 * (m + 1)], b1_sb[:, m:m + 1])
                    last.then_inc(h1_a, 1)
                elif kind == "layer2":
                    if n >= 1:
                        act.wait_ge(layer3_done, n)
                    act.wait_ge(layer2_a, n + 1)
                    act_relu(h2[:, 0, :], acc_ps[:, 0, 0:TILE], b2_sb[:, 0:1]).then_inc(h2_a, 1)
                elif kind == "layer3":
                    y_out_of_psum(n)
                elif kind == "last_tile":
                    act.wait_ge(layer2_b, n)
                    for i, m in enumerate((0, 2)):
                        act.wait_ge(layer1_a, n + 1 + i)
                        act_relu(h1[:, m, :], last_h1_ps(m), b1_sb[:, m:m + 1]).then_inc(h1_a, 1)
                    act.wait_ge(layer3_done, n)
                    act.wait_ge(layer2_a, n + 1)
                    act_relu(h2[:, 0, :], dots_ps[:, 0, 0:TILE], b2_sb[:, 0:1]).then_inc(h2_a, 1)
                    y_out_of_psum(n)

        @block.tensor
        def _(pe):
            def layer1(n, m, out):
                for t in range(STEPS):
                    last = nc.tensor.matmul(out, w1_sb[:, t, 128 * m:128 * (m + 1)], dots[:, t, n * TILE:(n + 1) * TILE],
                                            start=t == 0, stop=t == STEPS - 1)
                return last

            def layer2(k, m, out):
                return nc.tensor.matmul(out, w2_sb[:, k, 128 * m:128 * (m + 1)], h1[:, k, :], start=k == 0, stop=k == CHUNKS1 - 1)

            def layer3(n):
                for k in range(CHUNKS2):
                    pe.wait_ge((h2_a, h2_b)[k], n + 1)
                    last = nc.tensor.matmul(acc_ps[0:1, 0, 0:TILE], w3_sb[:, k:k + 1], h2[:, k, :], start=k == 0, stop=k == CHUNKS2 - 1)
                last.then_inc(layer3_done, 1)

            def tile_dots_out(n):
                pe.wait_ge(dots_out_act, DOTS_OUTS * GROUPS_PER_TILE * (n + 1))
                pe.wait_ge(dots_out_dve, DOTS_OUTS * GROUPS_PER_TILE * (n + 1))
                if n >= 1:
                    pe.wait_ge(y_ready, n)
                    pe.wait_ge(h2_b, n)

            def keep_warm(products):
                for _ in range(products):
                    nc.tensor.matmul(turn_ps[:, 1, 0:128], ident[:, :], ident[:, :], start=True, stop=True)

            pe.wait_ge(ident_ready, 2)
            keep_warm(11)
            for kind, n in pe_order:
                if kind == "pick":
                    pe.wait_ge(hi_ready, n + 1)
                    if n >= 1:
                        pe.wait_ge(lo_ready, n + 1)
                    if n >= 2:
                        pe.wait_ge(pick_out, n - 1)
                    passes = [[(tab_hi, c)] for c in range(PICK_CHUNKS)] + [[(tab_lo, c)] for c in range(PICK_CHUNKS)]
                    if n >= 1:
                        passes = [[(tab_hi, c), (tab_lo, c)] for c in range(PICK_CHUNKS)]
                    for products in passes:
                        for part, c in products:
                            if part is tab_hi:
                                if c < DVE_CHUNKS:
                                    pe.wait_ge(onehot_ready, n * DVE_CHUNKS + c + 1)
                                else:
                                    pe.wait_ge(last_onehot_ready, n + 1)
                            elif n == 0 and c == 0:
                                pe.wait_ge(lo_ready, 1)
                            last = nc.tensor.matmul(acc_ps[:, n % 2, :], part[0:PICK_K, n % TABLE_RING, EMBED * c:EMBED * (c + 1)],
                                                    onehot[0:PICK_K, (n * PICK_CHUNKS + c) % ONEHOT_RING, :],
                                                    start=part is tab_hi and c == 0,
                                                    stop=part is tab_lo and c == PICK_CHUNKS - 1)
                        if part is tab_lo:
                            last.then_inc(onehot_used, 1)
                elif kind == "turn":
                    fetches = FETCHES * (n // RAW_RING + 1) - (n == GROUPS - 1)
                    pe.wait_ge(raw_in[n % RAW_RING], 16 * fetches)
                    if n >= 1:
                        pe.wait_ge(turn_out_a, n)
                    for k in range(FETCHES):
                        if k == FIRST_FETCHES and n >= 1:
                            pe.wait_ge(turn_out_b, n)
                        if (n, k) == (GROUPS - 1, FETCHES - 1):
                            pe.wait_ge(last_raw_in, 16)
                        bank, at = (0, k) if k < FIRST_FETCHES else (1, k - FIRST_FETCHES)
                        last = nc.tensor.transpose(turn_ps[:, bank, 128 * at:128 * (at + 1)], raw[:, n % RAW_RING, k, :], ident[:, :])
                        if k == FIRST_FETCHES - 1:
                            last.then_inc(turned_a, 1)
                    last.then_inc(turned_b, 1)
                elif kind == "dots":
                    if n == 0:
                        pe.wait_ge(pad_zero, 1)
                        pe.wait_ge(pick_out, PICKS)
                    pe.wait_ge(turn_out_a, n + 1)
                    pe.wait_ge(turn_out_b, n + 1)
                    if n >= 2:
                        pe.wait_ge(dots_out_act, DOTS_OUTS * (n - 1))
                        pe.wait_ge(dots_out_dve, DOTS_OUTS * (n - 1))
                    for q in range(SETS):
                        at = n * GROUP + SET * q
                        bank = 2 * (n % 2) + q // 4
                        last = nc.tensor.matmul(dots_ps[:, bank, COLS * (q % 4):COLS * (q % 4 + 1)],
                                                emb[:, at:at + SET, :].rearrange("p s f -> p (s f)"),
                                                emb[:, at:at + SET, 0:FEATURES], start=True, stop=True)
                    last.then_inc(dotted, 1)
                elif kind == "layer1_first":
                    tile_dots_out(n)
                    if n == 0:
                        pe.wait_ge(w1_in, 16)
                        pe.wait_ge(dense_in, 16)
                    for m in (0, 1):
                        last = layer1(n, m, acc_ps[:, 0, 128 * m:128 * (m + 1)])
                    last.then_inc(layer1_a, 1)
                elif kind == "layer1_second":
                    for m in (2, 3):
                        last = layer1(n, m, acc_ps[:, 1, 128 * (m - 2):128 * (m - 1)])
                    last.then_inc(layer1_b, 1)
                elif kind == "layer2":
                    pe.wait_ge(h1_a, n + 1)
                    if n == 0:
                        pe.wait_ge(w23_in, 64)
                    for m in range(CHUNKS2):
                        for k in range(CHUNKS1):
                            if m == 0 and k == 2:
                                pe.wait_ge(h1_b, n + 1)
                            last = layer2(k, m, acc_ps[:, m, 0:TILE])
                        last.then_inc((layer2_a, layer2_b)[m], 1)
                elif kind == "layer3":
                    layer3(n)
                else:
                    keep_warm(9)
                    tile_dots_out(n)
                    for m in range(CHUNKS1):
                        layer1(n, m, last_h1_ps(m)).then_inc((layer1_a, layer1_b)[m % 2], 1)
                    for k in range(CHUNKS1):
                        pe.wait_ge((h1_a, h1_b)[k % 2], n + 1 + k // 2)
                        for m in range(CHUNKS2):
                            last = layer2(k, m, dots_ps[:, m, 0:TILE])
                            if k == CHUNKS1 - 1:
                                last.then_inc((layer2_a, layer2_b)[m], 1)
                    layer3(n)


def kernel(**inputs):
    import concourse.bacc as bacc
    from concourse import mybir
    from concourse.bass_utils import run_bass_kernel_spmd

    tables = [np.ascontiguousarray(inputs[f"tbl_{f}"]) for f in range(FEATURES)]
    ids = np.ascontiguousarray(inputs["ids"])
    fetch_ids = ids[:, FETCHED].reshape(GROUPS, GROUP, FETCHES, PER_FETCH).transpose(3, 1, 0, 2).reshape(128, -1)
    starts = np.concatenate([[0], np.cumsum([TABLE_ROWS[f] for f in FETCHED])[:-1]]).astype(np.int32)
    base = np.broadcast_to(starts.reshape(1, 1, FETCHES, PER_FETCH), (GROUPS, GROUP, FETCHES, PER_FETCH))
    pick_rows = np.arange(128 * PICK_CHUNKS, dtype=np.int32).reshape(128, PICK_CHUNKS)
    W1 = np.ascontiguousarray(inputs["W_top1"])
    w1 = np.zeros((4, QUAD, STEPS, HID1), W1.dtype)
    for i in range(FEATURES):
        for c, (k0, k1) in enumerate(QUAD_PLACES):
            for k in range(k0, k1):
                j = (i // BLOCK * BLOCK + 1 + k) % FEATURES
                if j // BLOCK != i // BLOCK or j > i:
                    lo, hi = sorted((SLOTS[i], SLOTS[j]))
                    w1[c, i, k - k0] = W1[hi * (hi - 1) // 2 + lo]
    w1[DENSE_QUAD, 0:DENSE, DENSE_STEP] = W1[FEATURES * (FEATURES - 1) // 2:]
    arrays = {
        "table": np.concatenate([tables[f] for f in FETCHED]),
        "fetch_ids": np.concatenate([fetch_ids, base.transpose(3, 1, 0, 2).reshape(128, -1), pick_rows], axis=1),
        "pick_ids": ids[:, PICKED].T,
        **{f"pick_table{n}": tables[f] for n, f in enumerate(PICKED)},
        "dense": inputs["dense_ctx"].T,
        "w1": w1.reshape(128, STEPS, HID1),
        "b1": inputs["b_top1"].reshape(CHUNKS1, 128).T,
        "w2": inputs["W_top2"],
        "b2": inputs["b_top2"].reshape(CHUNKS2, 128).T,
        "w3": inputs["W_top3"].reshape(CHUNKS2, 128).T,
    }
    arrays = {k: np.ascontiguousarray(a) for k, a in arrays.items()}
    nc = bacc.Bacc("TRN2", target_bir_lowering=False, num_devices=1)
    ap = {k: nc.dram_tensor(f"in_{k}", a.shape, mybir.dt.from_np(a.dtype), kind="ExternalInput").ap() for k, a in arrays.items()}
    y = nc.dram_tensor("out_y", (1, BATCH), mybir.dt.float32, kind="ExternalOutput").ap()
    build(nc, ap["table"], ap["fetch_ids"], ap["pick_ids"], [ap[f"pick_table{n}"] for n in range(PICKS)],
          ap["dense"], ap["w1"], ap["b1"], ap["w2"], ap["b2"], ap["w3"], y)
    r = run_bass_kernel_spmd(nc, [{f"in_{k}": a for k, a in arrays.items()}], core_ids=[0])
    return r.results[0]["out_y"].reshape(BATCH, 1)
```
